# Optimizing a Trainium2 kernel written in Bass

```python
import numpy as np
import jax
import jax.numpy as jnp

def _softmax(x, axis=-1):
    return jax.nn.softmax(x, axis=axis)

def _gelu(x):
    return jax.nn.gelu(x, approximate=True)

def _silu(x):
    return jax.nn.silu(x)

def _sigmoid(x):
    return jax.nn.sigmoid(x)

def _layernorm(x, axis=-1, eps=1e-05):
    m = jnp.mean(x, axis=axis, keepdims=True)
    v = jnp.var(x, axis=axis, keepdims=True)
    return (x - m) / jnp.sqrt(v + eps)

def _scatter_add(tgt, idx, src, axis=0):
    return tgt.at[idx].add(src)

def _segment_sum(src, seg, n):
    return jax.ops.segment_sum(src, seg, n)
kernel_name = 'mk_seq_postln_d1_jaxref_r8_ac1e08'

def setup_inputs(seed: int=0):
    np.random.seed(seed)
    _w = jnp.asarray

    def _L0_attn_setup():
        import jax, jax.numpy as jnp
        import numpy as np
        D_MODEL = 128
        EXPAND = 2
        D_INNER = D_MODEL * EXPAND
        D_STATE = 16
        D_CONV = 4
        DT_RANK = max(16, D_MODEL // 16)
        BATCH = 1
        SEQ = 256

        def _hippo_eigvals(N):
            n = np.arange(N)
            A = -(2.0 * np.maximum(n[:, None], n[None, :]) + 1.0)
            w, _ = np.linalg.eigh(A)
            idx = np.argsort(np.abs(w))[::-1]
            return w[idx]
        key = jax.random.key(seed)
        ks = jax.random.split(key, 10)
        s = 0.02
        return {'x': jax.random.normal(ks[0], (BATCH, SEQ, D_MODEL), jnp.float32), 'in_w': jax.random.normal(ks[1], (D_MODEL, D_INNER), jnp.float32) * s, 'in_b': jnp.zeros((D_INNER,), jnp.float32), 'conv_w': jax.random.normal(ks[2], (D_INNER, 1, D_CONV), jnp.float32) * s, 'conv_b': jnp.zeros((D_INNER,), jnp.float32), 'A_log': jnp.asarray(np.log(np.abs(_hippo_eigvals(D_STATE))), jnp.float32), 'B_mat': jax.random.normal(ks[3], (D_STATE, D_INNER), jnp.float32) * s, 'C_mat': jax.random.normal(ks[4], (D_STATE, D_INNER), jnp.float32) * s, 'D_vec': jnp.ones((D_INNER,), jnp.float32), 'gate_w': jax.random.normal(ks[5], (D_MODEL, D_INNER), jnp.float32) * s, 'gate_b': jnp.zeros((D_INNER,), jnp.float32), 'dt1_w': jax.random.normal(ks[6], (D_INNER, DT_RANK), jnp.float32) * s, 'dt1_b': jnp.zeros((DT_RANK,), jnp.float32), 'dt2_w': jax.random.normal(ks[7], (DT_RANK, D_INNER), jnp.float32) * s, 'dt2_b': jnp.full((D_INNER,), -4.0, jnp.float32), 'out_w': jax.random.normal(ks[8], (D_INNER, D_MODEL), jnp.float32) * s, 'out_b': jnp.zeros((D_MODEL,), jnp.float32)}
    _L0_attn_in = _L0_attn_setup()

    def _L0_ffn_setup():
        import jax, jax.numpy as jnp
        import numpy as np
        DIM = 128
        DEPTH = 2
        HEADS = 8
        DIM_HEAD = 64
        WINDOW = 64
        INNER = HEADS * DIM_HEAD
        HID = int(DIM * 4 * 2 / 3)
        B, N = (2, 1024)
        QK_SCALE = 8.0

        def shift_token(t):
            t1, t2 = jnp.split(t, 2, axis=-1)
            t2 = jnp.pad(t2, ((0, 0), (1, 0), (0, 0)))[:, :-1]
            return jnp.concatenate([t1, t2], axis=-1)

        def l2norm(t):
            return t / jnp.clip(jnp.linalg.norm(t, axis=-1, keepdims=True), 1e-12)

        def rotate_half(x):
            x1, x2 = jnp.split(x, 2, axis=-1)
            return jnp.concatenate([-x2, x1], axis=-1)

        def rotary_xpos(q, k):
            n = q.shape[-2]
            half_idx = jnp.arange(0, DIM_HEAD, 2, dtype=jnp.float32)
            inv_freq = 1.0 / 10000.0 ** (half_idx / DIM_HEAD)
            t = jnp.arange(n, dtype=jnp.float32)
            freqs = t[:, None] * inv_freq[None, :]
            freqs = jnp.concatenate([freqs, freqs], axis=-1)
            base = (half_idx + 0.4 * DIM_HEAD) / (1.4 * DIM_HEAD)
            power = (t - n // 2) / float(WINDOW // 2)
            scale = base[None, :] ** power[:, None]
            scale = jnp.concatenate([scale, scale], axis=-1)
            cos, sin = (jnp.cos(freqs), jnp.sin(freqs))
            q = q * cos * scale + rotate_half(q) * sin * scale
            k = k * cos / scale + rotate_half(k) * sin / scale
            return (q, k)

        def local_attention(q, k, v):
            b, h, n, d = q.shape
            w = n // WINDOW
            bq = q.reshape(b, h, w, WINDOW, d) * QK_SCALE
            bk = k.reshape(b, h, w, WINDOW, d)
            bv = v.reshape(b, h, w, WINDOW, d)

            def look_around(t):
                p = jnp.pad(t, ((0, 0), (0, 0), (1, 0), (0, 0), (0, 0)))
                return jnp.concatenate([p[:, :, :w], p[:, :, 1:]], axis=3)
            bk, bv = (look_around(bk), look_around(bv))
            bt = jnp.arange(n).reshape(w, WINDOW)
            btp = jnp.pad(bt, ((1, 0), (0, 0)), constant_values=-1)
            btk = jnp.concatenate([btp[:w], btp[1:]], axis=1)
            sim = jnp.einsum('bhwid,bhwjd->bhwij', bq, bk)
            i = bt[:, :, None]
            j = btk[:, None, :]
            mask = (i < j) | (i > j + WINDOW) | (j == -1)
            sim = jnp.where(mask, -jnp.finfo(sim.dtype).max, sim)
            attn = jax.nn.softmax(sim, axis=-1)
            out = jnp.einsum('bhwij,bhwjd->bhwid', attn, bv)
            return out.reshape(b, h, n, d)

        def _layer(x, wqkv, qs, ksc, wo, lg, lb, w1, b1, w2, b2):
            b, n, _ = x.shape
            h = shift_token(x)
            qkv = h @ wqkv
            q, k, v = jnp.split(qkv, 3, axis=-1)
            to_heads = lambda t: t.reshape(b, n, HEADS, DIM_HEAD).transpose(0, 2, 1, 3)
            q, k, v = (to_heads(q), to_heads(k), to_heads(v))
            q = l2norm(q) * qs
            k = l2norm(k) * ksc
            q, k = rotary_xpos(q, k)
            o = local_attention(q, k, v)
            o = o.transpose(0, 2, 1, 3).reshape(b, n, INNER)
            x = x + o @ wo
            h = shift_token(x)
            mu = h.mean(-1, keepdims=True)
            var = h.var(-1, keepdims=True)
            h = (h - mu) / jnp.sqrt(var + 1e-05) * lg + lb
            h = h @ w1 + b1
            a, g = jnp.split(h, 2, axis=-1)
            h = a * jax.nn.gelu(g, approximate=False)
            x = x + h @ w2 + b2
            return x
        key = jax.random.key(seed)
        ks = jax.random.split(key, 6)
        return {'x': jax.random.normal(ks[0], (B, N, DIM), jnp.float32), 'wqkv': jax.random.normal(ks[1], (DEPTH, DIM, 3 * INNER), jnp.float32) * 0.02, 'q_scale': jnp.ones((DEPTH, DIM_HEAD), jnp.float32), 'k_scale': jnp.ones((DEPTH, DIM_HEAD), jnp.float32), 'wo': jax.random.normal(ks[2], (DEPTH, INNER, DIM), jnp.float32) * 0.02, 'ln_g': jnp.ones((DEPTH, DIM), jnp.float32), 'ln_b': jnp.zeros((DEPTH, DIM), jnp.float32), 'w1': jax.random.normal(ks[3], (DEPTH, DIM, 2 * HID), jnp.float32) * 0.02, 'b1': jnp.zeros((DEPTH, 2 * HID), jnp.float32), 'w2': jax.random.normal(ks[4], (DEPTH, HID, DIM), jnp.float32) * 0.02, 'b2': jnp.zeros((DEPTH, DIM), jnp.float32)}
    _L0_ffn_in = _L0_ffn_setup()
    _d = {'L0_attn_x': _L0_attn_in['x'], 'L0_attn_in_w': _L0_attn_in['in_w'], 'L0_attn_in_b': _L0_attn_in['in_b'], 'L0_attn_conv_w': _L0_attn_in['conv_w'], 'L0_attn_conv_b': _L0_attn_in['conv_b'], 'L0_attn_A_log': _L0_attn_in['A_log'], 'L0_attn_B_mat': _L0_attn_in['B_mat'], 'L0_attn_C_mat': _L0_attn_in['C_mat'], 'L0_attn_D_vec': _L0_attn_in['D_vec'], 'L0_attn_gate_w': _L0_attn_in['gate_w'], 'L0_attn_gate_b': _L0_attn_in['gate_b'], 'L0_attn_dt1_w': _L0_attn_in['dt1_w'], 'L0_attn_dt1_b': _L0_attn_in['dt1_b'], 'L0_attn_dt2_w': _L0_attn_in['dt2_w'], 'L0_attn_dt2_b': _L0_attn_in['dt2_b'], 'L0_attn_out_w': _L0_attn_in['out_w'], 'L0_attn_out_b': _L0_attn_in['out_b'], 'L0_ffn_wqkv': _L0_ffn_in['wqkv'], 'L0_ffn_q_scale': _L0_ffn_in['q_scale'], 'L0_ffn_k_scale': _L0_ffn_in['k_scale'], 'L0_ffn_wo': _L0_ffn_in['wo'], 'L0_ffn_ln_g': _L0_ffn_in['ln_g'], 'L0_ffn_ln_b': _L0_ffn_in['ln_b'], 'L0_ffn_w1': _L0_ffn_in['w1'], 'L0_ffn_b1': _L0_ffn_in['b1'], 'L0_ffn_w2': _L0_ffn_in['w2'], 'L0_ffn_b2': _L0_ffn_in['b2']}
    _x0 = _d['L0_attn_x']
    _d['L0_attn_x'] = jax.random.normal(jax.random.fold_in(jax.random.key(seed), 1), (16, 256, 128), dtype=_x0.dtype)
    del _x0
    return _d

def reference(L0_attn_x, L0_attn_in_w, L0_attn_in_b, L0_attn_conv_w, L0_attn_conv_b, L0_attn_A_log, L0_attn_B_mat, L0_attn_C_mat, L0_attn_D_vec, L0_attn_gate_w, L0_attn_gate_b, L0_attn_dt1_w, L0_attn_dt1_b, L0_attn_dt2_w, L0_attn_dt2_b, L0_attn_out_w, L0_attn_out_b, L0_ffn_wqkv, L0_ffn_q_scale, L0_ffn_k_scale, L0_ffn_wo, L0_ffn_ln_g, L0_ffn_ln_b, L0_ffn_w1, L0_ffn_b1, L0_ffn_w2, L0_ffn_b2):

    def _L0_attn_ref(x, in_w, in_b, conv_w, conv_b, A_log, B_mat, C_mat, D_vec, gate_w, gate_b, dt1_w, dt1_b, dt2_w, dt2_b, out_w, out_b):
        import jax, jax.numpy as jnp
        import numpy as np
        D_MODEL = 128
        EXPAND = 2
        D_INNER = D_MODEL * EXPAND
        D_STATE = 16
        D_CONV = 4
        DT_RANK = max(16, D_MODEL // 16)
        BATCH = 1
        SEQ = 256

        def _hippo_eigvals(N):
            n = np.arange(N)
            A = -(2.0 * np.maximum(n[:, None], n[None, :]) + 1.0)
            w, _ = np.linalg.eigh(A)
            idx = np.argsort(np.abs(w))[::-1]
            return w[idx]
        B, L, _ = x.shape
        u = x @ in_w + in_b
        uc = jax.lax.conv_general_dilated(u.transpose(0, 2, 1), conv_w, (1,), [(D_CONV - 1, 0)], dimension_numbers=('NCH', 'OIH', 'NCH'), feature_group_count=D_INNER) + conv_b[None, :, None]
        u = jax.nn.silu(uc.transpose(0, 2, 1))
        delta = jax.nn.softplus((u @ dt1_w + dt1_b) @ dt2_w + dt2_b)
        A = -jnp.exp(A_log)
        dA = delta[..., None] * A
        A_bar = jnp.exp(dA)
        safe_A = jnp.where(jnp.abs(A) < 1e-06, 1.0, A)
        expansion = jnp.where(jnp.abs(A) < 1e-06, delta[..., None] * (1.0 + 0.5 * dA), (A_bar - 1.0) / safe_A)
        Bu = expansion * B_mat.T[None, None, :, :] * u[..., None]

        def step(h, ab_bu):
            ab, bu = ab_bu
            h = ab * h + bu
            return (h, h)
        h0 = jnp.zeros((B, D_INNER, D_STATE), x.dtype)
        _, hs = jax.lax.scan(step, h0, (A_bar.transpose(1, 0, 2, 3), Bu.transpose(1, 0, 2, 3)))
        hs = hs.transpose(1, 0, 2, 3)
        y = jnp.einsum('bldn,nd->bld', hs, C_mat) + D_vec * u
        y = y * jax.nn.silu(x @ gate_w + gate_b)
        return y @ out_w + out_b

    def _L0_ffn_ref(x, wqkv, q_scale, k_scale, wo, ln_g, ln_b, w1, b1, w2, b2):
        import jax, jax.numpy as jnp
        import numpy as np
        DIM = 128
        DEPTH = 2
        HEADS = 8
        DIM_HEAD = 64
        WINDOW = 64
        INNER = HEADS * DIM_HEAD
        HID = int(DIM * 4 * 2 / 3)
        B, N = (2, 1024)
        QK_SCALE = 8.0

        def shift_token(t):
            t1, t2 = jnp.split(t, 2, axis=-1)
            t2 = jnp.pad(t2, ((0, 0), (1, 0), (0, 0)))[:, :-1]
            return jnp.concatenate([t1, t2], axis=-1)

        def l2norm(t):
            return t / jnp.clip(jnp.linalg.norm(t, axis=-1, keepdims=True), 1e-12)

        def rotate_half(x):
            x1, x2 = jnp.split(x, 2, axis=-1)
            return jnp.concatenate([-x2, x1], axis=-1)

        def rotary_xpos(q, k):
            n = q.shape[-2]
            half_idx = jnp.arange(0, DIM_HEAD, 2, dtype=jnp.float32)
            inv_freq = 1.0 / 10000.0 ** (half_idx / DIM_HEAD)
            t = jnp.arange(n, dtype=jnp.float32)
            freqs = t[:, None] * inv_freq[None, :]
            freqs = jnp.concatenate([freqs, freqs], axis=-1)
            base = (half_idx + 0.4 * DIM_HEAD) / (1.4 * DIM_HEAD)
            power = (t - n // 2) / float(WINDOW // 2)
            scale = base[None, :] ** power[:, None]
            scale = jnp.concatenate([scale, scale], axis=-1)
            cos, sin = (jnp.cos(freqs), jnp.sin(freqs))
            q = q * cos * scale + rotate_half(q) * sin * scale
            k = k * cos / scale + rotate_half(k) * sin / scale
            return (q, k)

        def local_attention(q, k, v):
            b, h, n, d = q.shape
            w = n // WINDOW
            bq = q.reshape(b, h, w, WINDOW, d) * QK_SCALE
            bk = k.reshape(b, h, w, WINDOW, d)
            bv = v.reshape(b, h, w, WINDOW, d)

            def look_around(t):
                p = jnp.pad(t, ((0, 0), (0, 0), (1, 0), (0, 0), (0, 0)))
                return jnp.concatenate([p[:, :, :w], p[:, :, 1:]], axis=3)
            bk, bv = (look_around(bk), look_around(bv))
            bt = jnp.arange(n).reshape(w, WINDOW)
            btp = jnp.pad(bt, ((1, 0), (0, 0)), constant_values=-1)
            btk = jnp.concatenate([btp[:w], btp[1:]], axis=1)
            sim = jnp.einsum('bhwid,bhwjd->bhwij', bq, bk)
            i = bt[:, :, None]
            j = btk[:, None, :]
            mask = (i < j) | (i > j + WINDOW) | (j == -1)
            sim = jnp.where(mask, -jnp.finfo(sim.dtype).max, sim)
            attn = jax.nn.softmax(sim, axis=-1)
            out = jnp.einsum('bhwij,bhwjd->bhwid', attn, bv)
            return out.reshape(b, h, n, d)

        def _layer(x, wqkv, qs, ksc, wo, lg, lb, w1, b1, w2, b2):
            b, n, _ = x.shape
            h = shift_token(x)
            qkv = h @ wqkv
            q, k, v = jnp.split(qkv, 3, axis=-1)
            to_heads = lambda t: t.reshape(b, n, HEADS, DIM_HEAD).transpose(0, 2, 1, 3)
            q, k, v = (to_heads(q), to_heads(k), to_heads(v))
            q = l2norm(q) * qs
            k = l2norm(k) * ksc
            q, k = rotary_xpos(q, k)
            o = local_attention(q, k, v)
            o = o.transpose(0, 2, 1, 3).reshape(b, n, INNER)
            x = x + o @ wo
            h = shift_token(x)
            mu = h.mean(-1, keepdims=True)
            var = h.var(-1, keepdims=True)
            h = (h - mu) / jnp.sqrt(var + 1e-05) * lg + lb
            h = h @ w1 + b1
            a, g = jnp.split(h, 2, axis=-1)
            h = a * jax.nn.gelu(g, approximate=False)
            x = x + h @ w2 + b2
            return x
        for l in range(DEPTH):
            x = _layer(x, wqkv[l], q_scale[l], k_scale[l], wo[l], ln_g[l], ln_b[l], w1[l], b1[l], w2[l], b2[l])
        return x
    x = L0_attn_x
    x = _layernorm(x + _L0_attn_ref(x, L0_attn_in_w, L0_attn_in_b, L0_attn_conv_w, L0_attn_conv_b, L0_attn_A_log, L0_attn_B_mat, L0_attn_C_mat, L0_attn_D_vec, L0_attn_gate_w, L0_attn_gate_b, L0_attn_dt1_w, L0_attn_dt1_b, L0_attn_dt2_w, L0_attn_dt2_b, L0_attn_out_w, L0_attn_out_b), axis=-1)
    x = _layernorm(x + _L0_ffn_ref(x, L0_ffn_wqkv, L0_ffn_q_scale, L0_ffn_k_scale, L0_ffn_wo, L0_ffn_ln_g, L0_ffn_ln_b, L0_ffn_w1, L0_ffn_b1, L0_ffn_w2, L0_ffn_b2), axis=-1)
    return x

_drawn_inputs = setup_inputs


def setup_inputs(seed=0):
    import zlib

    import numpy as np

    out = dict(_drawn_inputs(seed))
    spreads = {'L0_attn_in_b': (0.0, 0.8),
     'L0_attn_conv_b': (0.0, 0.8),
     'L0_attn_D_vec': (1.0, 0.6),
     'L0_attn_gate_b': (0.0, 0.8),
     'L0_attn_dt1_b': (0.0, 0.8),
     'L0_attn_dt2_b': (-4.0, 0.6),
     'L0_attn_out_b': (0.0, 0.1),
     'L0_ffn_q_scale': (1.0, 0.6),
     'L0_ffn_k_scale': (1.0, 0.6),
     'L0_ffn_ln_g': (1.0, 0.6),
     'L0_ffn_ln_b': (0.0, 0.8),
     'L0_ffn_b1': (0.0, 0.8),
     'L0_ffn_b2': (0.0, 0.548)}
    factors = {'L0_attn_in_w': 8.0,
     'L0_attn_conv_w': 8.0,
     'L0_attn_A_log': 8.0,
     'L0_attn_B_mat': 8.0,
     'L0_attn_C_mat': 8.0,
     'L0_attn_gate_w': 8.0,
     'L0_attn_dt1_w': 8.0,
     'L0_attn_dt2_w': 8.0,
     'L0_attn_out_w': 8.0,
     'L0_ffn_wqkv': 3.262,
     'L0_ffn_wo': 3.207,
     'L0_ffn_w1': 6.207,
     'L0_ffn_w2': 6.137}
    for name, (base, spread) in spreads.items():
        noise = np.random.default_rng([zlib.crc32(name.encode()), seed]).standard_normal(out[name].shape)
        drawn = base * np.exp(spread * noise) if base else spread * noise
        out[name] = jnp.asarray(drawn.astype(out[name].dtype))
    for name, factor in factors.items():
        out[name] = (out[name] * factor).astype(out[name].dtype)
    return out
```

```python
from contextlib import ExitStack

import concourse.bass as bass
from concourse import mybir

F32 = mybir.dt.float32
BF16 = mybir.dt.bfloat16
ALU = mybir.AluOpType
ACT = mybir.ActivationFunctionType
AX = mybir.AxisListType

P = 128
D = 128
DI = 256
HALF = DI // P
NST = 16
RANK = 16
TAPS = 4
BATCH, SEQ = 16, 256
SEQS = 2
GROUPS = BATCH // SEQS
TOK = SEQS * SEQ
TILES = TOK // P
SEQP = SEQ + 1
LAYERS, HEADS, DH, WIN = 2, 8, 64, 64
INNER = HEADS * DH
PAIRS = HEADS // 2
HID = int(D * 4 * 2 / 3)
CH = [(0, 128), (128, 128), (256, HID - 256)]
NCH = len(CH)
QK_SCALE = 8.0
EPS = 1e-5
A_RING = 3
R_RING = 3
MASKED = -3.0e38
TINY_A = 1e-6

PV = {}
PV_COLS = 0
for _name, _n in (("in_b", HALF), ("gate_b", HALF), ("conv_b", HALF), ("conv_w", HALF * TAPS),
                  ("D", HALF), ("dt1_b", 1), ("dt2_b", HALF), ("B", HALF * NST), ("C", HALF * NST),
                  ("ln_g", LAYERS), ("ln_b", LAYERS), ("b1a", LAYERS * NCH), ("b1g", LAYERS * NCH)):
    PV[_name] = PV_COLS
    PV_COLS += _n
BV = {}
BV_COLS = 0
for _name, _n in (("A_log", NST), ("out_b", D), ("qk_scale", LAYERS * 2 * DH), ("b2", LAYERS * D)):
    BV[_name] = BV_COLS
    BV_COLS += _n


def order():
    yield "mamba", "enter", ()
    for l in range(LAYERS):
        yield "ffn", "layer_in", (l,)
        for s in range(TILES + 2):
            yield "ffn", "slot", (l, s)
            if l == 0:
                if s == 0:
                    yield "mamba", "activate", ()
                elif s == 1:
                    yield "mamba", "rank", ()
                elif s == 2:
                    yield "mamba", "step_size", ()
                elif s == 3:
                    yield "mamba", "skip", ()
            at = SCANS_AT[l][s]
            for n in range(at[0], at[1]):
                yield "mamba", "state", (n,)
        yield "ffn", "attn_out", (l,)
        for n in range(*SCANS_AT[l][TILES + 2]):
            yield "mamba", "state", (n,)
        yield "ffn", "ffn", (l,)
        for n in range(*SCANS_AT[l][TILES + 3]):
            yield "mamba", "state", (n,)
    yield "ffn", "final", ()
    yield "mamba", "leave", ()


def _spread():
    counts = [[0, 0, 0, 1, 1, 1, 1, 1], [1, 1, 1, 1, 2, 2, 2, 1]]
    at, out = 0, []
    for row in counts:
        out.append([])
        for c in row:
            out[-1].append((at, at + c))
            at += c
    assert at == NST
    return out


SCANS_AT = _spread()


def build(nc, t, out):
    with ExitStack() as ctx:
        def sb(name, shape, dt=F32):
            return ctx.enter_context(nc.sbuf_tensor(name, shape, dt))

        per_group = {}

        def signal(name, per=1):
            semaphore = ctx.enter_context(nc.semaphore(name))
            per_group[id(semaphore)] = per
            return semaphore

        def at(semaphore, g, n=None):
            per = per_group[id(semaphore)]
            return g * per + (per if n is None else n)

        in_w = sb("in_w", [P, DI])
        gate_w = sb("gate_w", [P, DI])
        dt1_w = sb("dt1_w", [P, HALF, RANK])
        dt2_w = sb("dt2_w", [RANK, DI])
        out_w = sb("out_w", [P, HALF, D])
        wqkv = sb("wqkv", [P, LAYERS, 3 * INNER])
        wo = sb("wo", [P, LAYERS, INNER // P, D])
        w1 = sb("w1", [P, LAYERS, 2 * HID])
        w2 = sb("w2", [P, LAYERS, NCH, D])
        pv = sb("pv", [P, PV_COLS])
        bv = sb("bv", [P, BV_COLS])
        ident = sb("ident", [P, P])
        identb = sb("identb", [P, P], BF16)
        shift = sb("shift", [P, P])
        carry = sb("carry", [P, P])
        mask = sb("mask", [P, 2, P], BF16)
        rope_c = sb("rope_c", [P, LAYERS, 2, 2, DH])
        rope_s = sb("rope_s", [P, LAYERS, 2, 2, DH])
        diag = sb("diag", [P, HALF, NST + 1, P])
        negA = sb("negA", [P, NST])
        rA = sb("rA", [P, NST])
        halfA = sb("halfA", [P, NST])
        tiny = sb("tiny", [P, NST])
        keep = sb("keep", [P, NST])
        expand = sb("expand", [P, NST])
        any_tiny = sb("any_tiny", [P, 1])
        none_tiny = sb("none_tiny", [P, 1])
        flag = sb("flag", [P, 1], mybir.dt.int32)
        wsum = sb("wsum", [P, HALF, NST + 1])
        half_cw = sb("half_cw", [P, HALF * TAPS])
        half_cb = sb("half_cb", [P, HALF])
        half_gb = sb("half_gb", [P, HALF])
        zero = sb("zero", [P, D])
        tick = sb("tick", [P, 1])
        expo = sb("expo", [P, 64])

        xT = sb("xT", [P, TOK])
        xres = sb("xres", [P, TILES, D])
        upre = sb("upre", [P, HALF * SEQS, SEQ + TAPS - 1])
        hu = sb("hu", [P, HALF * SEQS, SEQ])
        th = sb("th", [P, HALF * SEQS, SEQ])
        gate = sb("gate", [P, HALF * SEQS, SEQ])
        u = sb("u", [P, HALF * SEQS, SEQP])
        du = sb("du", [P, HALF * SEQS, SEQP])
        delta = sb("delta", [P, HALF * SEQS, SEQ])
        dt1_s = sb("dt1_s", [RANK, TOK])
        decay = sb("decay", [P, A_RING, HALF * SEQS, SEQP])
        scan = sb("scan", [P, R_RING, HALF * SEQS, SEQP])
        x1 = sb("x1", [P, TILES, D])
        m_st = sb("m_st", [P, TILES, 6])
        m_mv = sb("m_mv", [P, TILES, 2])
        m_ve = sb("m_ve", [P, TILES])
        m_rs = sb("m_rs", [P, TILES])

        xf = sb("xf", [P, TILES, D])
        x1c = sb("x1c", [P, TILES, D])
        hT = sb("hT", [P, SEQS, SEQ])
        sq = sb("sq", [P, 2, INNER])
        qc = sb("qc", [P, 2, INNER])
        qs = sb("qs", [P, 2, INNER])
        qk = sb("qk", [P, 2, 2, INNER])
        ss = sb("ss", [P, 2 * HEADS])
        ssc = sb("ssc", [P, 2 * HEADS])
        rn = sb("rn", [P, 2 * HEADS])
        qT = sb("qT", [P, 2, PAIRS, P])
        kT = sb("kT", [P, SEQS, PAIRS, WIN + SEQ])
        v_odd = sb("v_odd", [P, TILES, INNER])
        v_even = sb("v_even", [P, TILES, INNER])
        nmax = sb("nmax", [P, 2, HEADS])
        den = sb("den", [P, 2, HEADS])
        rden = sb("rden", [P, HEADS])
        prob = sb("prob", [P, HEADS, P])
        probT = sb("probT", [P, HEADS, P])
        o_s = sb("o_s", [P, INNER])
        oT = sb("oT", [P, TILES, INNER // P, P])
        f_st = sb("f_st", [P, TILES, 2, 6])
        f_mv = sb("f_mv", [P, TILES, 2])
        f_ve = sb("f_ve", [P, TILES])
        f_rs = sb("f_rs", [P, TILES])
        hn = sb("hn", [P, TILES, D])
        hnT = sb("hnT", [P, TOK])
        hid = sb("hid", [P, NCH, TOK])
        outb = sb("outb", [P, TILES, D])

        Y = [ctx.enter_context(nc.psum_tensor(f"Y{i}", [P, TOK], F32)) for i in range(HALF)]
        M = ctx.enter_context(nc.psum_tensor("M", [P, TOK], F32))
        F = [ctx.enter_context(nc.psum_tensor(f"F{i}", [P, TOK], F32)) for i in range(5)]

        w_in = ctx.enter_context(nc.semaphore("weights_in"))
        out_done = ctx.enter_context(nc.semaphore("out_done"))
        xT_in = ctx.enter_context(nc.semaphore("xT_in"))
        xres_in = ctx.enter_context(nc.semaphore("xres_in"))
        expo_ready = signal("expo_ready")
        zeros_ready = signal("zeros_ready")
        a_exp = signal("a_exp")
        setup = signal("setup_steps")
        setup_done = signal("setup_done")

        u_ps = signal("u_ps", HALF)
        g_ps = signal("g_ps", HALF)
        upre_sb = signal("upre_sb", HALF)
        gh_sb = signal("gh_sb", HALF)
        conv = signal("conv_steps", HALF * TAPS)
        th_u = signal("th_u")
        u_sb = signal("u_sb")
        th_g = signal("th_g")
        gate_sb = signal("gate_sb")
        du_sb = signal("du_sb")
        d1_ps = signal("d1_ps")
        d1_sb = signal("d1_sb")
        z_ps = signal("z_ps", HALF)
        za_sb = signal("za_sb", HALF)
        zr_sb = signal("zr_sb", HALF)
        e_sb = signal("e_sb")
        l_sb = signal("l_sb")
        delta_sb = signal("delta_sb")
        decay_sb = signal("decay_sb", NST)
        scan_sb = signal("scan_sb", NST)
        series = signal("series_steps", 5 * NST)
        scan_used = signal("scan_used", NST - 1)
        y_ps = signal("y_ps", HALF)
        yg_sb = signal("yg_sb", HALF)
        mo_ps = signal("mo_ps")
        xb_sb = signal("xb_sb")
        m_sum = signal("m_sum")
        m_stat = signal("m_stat")
        m_aggr = signal("m_aggr")
        m_var = signal("m_var")
        m_rstd = signal("m_rstd")
        x1_sb = signal("x1_sb")
        x1_taken = signal("x1_taken", 2)

        TS = LAYERS * TILES
        ht_ps = signal("ht_ps", LAYERS)
        ht_sb = signal("ht_sb", LAYERS)
        qkv_ps = signal("qkv_ps", 3 * TS)
        sq_sb = signal("sq_sb", 2 * TS)
        v_sb = signal("v_sb", TS)
        ve_sb = signal("ve_sb", TS + TS // 2)
        ss_sb = signal("ss_sb", TS)
        ssc_sb = signal("ssc_sb", TS)
        rn_sb = signal("rn_sb", TS)
        rope_mul = signal("rope_mul", 2 * TS)
        rope_add = signal("rope_add", TS)
        qk_sb = signal("qk_sb", TS)
        qkT_ps = signal("qkT_ps", 2 * TS)
        qkT_sb = signal("qkT_sb", 2 * TS)
        s_ps = signal("s_ps", 2 * TS)
        nmax_sb = signal("nmax_sb", 2 * TS)
        prob_sb = signal("prob_sb", 2 * TS)
        rden_sb = signal("rden_sb", TS)
        pT_ps = signal("pT_ps", 2 * TS)
        pTe_sb = signal("pTe_sb", TS)
        pTo_sb = signal("pTo_sb", TS)
        o_ps = signal("o_ps", TS)
        o_sb = signal("o_sb", TS)
        oT_ps = signal("oT_ps", TS)
        oT_sb = signal("oT_sb", TS)
        wo_ps = signal("wo_ps", LAYERS)
        x2_sb = signal("x2_sb", LAYERS)
        xb2_sb = signal("xb2_sb", LAYERS)
        sh_ps = signal("sh_ps", LAYERS)
        f_stat = signal("f_stat", LAYERS)
        f_aggr = signal("f_aggr", LAYERS + 1)
        f_var = signal("f_var", LAYERS + 1)
        f_rstd = signal("f_rstd", LAYERS + 1)
        hn_sb = signal("hn_sb", LAYERS)
        hnT_ps = signal("hnT_ps", LAYERS)
        hnT_sb = signal("hnT_sb", LAYERS)
        up_ps = signal("up_ps", 2 * NCH * LAYERS)
        gelu_sb = signal("gelu_sb", NCH * LAYERS)
        hid_sb = signal("hid_sb", NCH * LAYERS)
        w2_ps = signal("w2_ps", LAYERS)
        x3_sb = signal("x3_sb", LAYERS)
        z_sum = signal("z_sum")
        z_stat = signal("z_stat")
        out_sb = signal("out_sb")

        def col(name, i=0, rows=P):
            return pv[0:rows, PV[name] + i:PV[name] + i + 1]

        def seqs(ap):
            return ap.rearrange("p (s l) -> p s l", s=SEQS)

        W_IN = [0]

        def run(eng, mamba, ffn):
            def turn(gm, gf):
                for who, step, args in order():
                    part, g = (mamba, gm) if who == "mamba" else (ffn, gf)
                    if g is not None and step in part:
                        part[step](g, *args)

            turn(0, None)
            with eng.Fori(1, GROUPS) as g:
                turn(g, g - 1)
            turn(None, GROUPS - 1)

        block = ctx.enter_context(nc.Block())

        @block.sync
        def _(sp):
            loads = [(in_w[:, :], t["in_w"]), (gate_w[:, :], t["gate_w"]),
                     (dt1_w[:, :, :], t["dt1_w"].rearrange("(h p) r -> p h r", h=HALF)),
                     (dt2_w[:, :], t["dt2_w"]),
                     (pv[:, :], t["pv"]), (bv[:, :], t["bv"].partition_broadcast(P)),
                     (ident[:, :], t["ident"]),
                     (shift[:, :], t["shift"]), (carry[:, :], t["carry"]),
                     (prob[:, 0:2, :], t["mask"]),
                     (rope_c[:, 0], t["rope_c"]), (rope_s[:, 0], t["rope_s"]),
                     (rope_c[:, 1], t["rope_c"]), (rope_s[:, 1], t["rope_s"]),
                     (out_w[:, :, :], t["out_w"].rearrange("(h p) n -> p h n", h=HALF)),
                     (wqkv[:, :, :], t["wqkv"].rearrange("l p n -> p l n")),
                     (wo[:, :, :, :], t["wo"].rearrange("l (c p) n -> p l c n", p=P)),
                     (w1[:, :, :], t["w1"].rearrange("l p n -> p l n"))]
            for l in range(LAYERS):
                loads.append((w2[:, l, 0:2, :], t["w2"][l, 0:2 * P, :].rearrange("(c p) n -> p c n", p=P)))
                loads.append((w2[0:CH[2][1], l, 2, :], t["w2"][l, 2 * P:HID, :]))
            for dst, src in loads:
                sp.dma_start(dst, src).then_inc(w_in, 16)
            W_IN[0] = 16 * len(loads)

            def load_x(g):
                sp.dma_start(xT[:, :], t["xT"][g]).then_inc(xT_in, 16)
                sp.dma_start(xres[:, :, :], t["x"][g].rearrange("(t p) d -> p t d", p=P)).then_inc(xres_in, 16)

            load_x(0)
            with sp.Fori(1, GROUPS) as g:
                sp.wait_ge(g_ps, at(g_ps, g, 0))
                sp.wait_ge(x1_sb, g)
                load_x(g)
                sp.wait_ge(out_sb, g)
                sp.dma_start(out[g - 1].rearrange("(t p) d -> p t d", p=P), outb[:, :, :]).then_inc(out_done, 16)
            sp.wait_ge(out_sb, at(out_sb, GROUPS - 1))
            sp.dma_start(out[GROUPS - 1].rearrange("(t p) d -> p t d", p=P), outb[:, :, :]).then_inc(out_done, 16)
            sp.wait_ge(out_done, 16 * (GROUPS + 1))

        @block.gpsimd
        def _(pool):
            pool.memset(expo[:, :], -0.5).then_inc(expo_ready, 1)
            pool.wait_ge(expo_ready, 1)
            pool.wait_ge(zeros_ready, 1)
            pool.wait_ge(w_in, W_IN[0])

            def bias(g):
                pool.wait_ge(xres_in, g * 16 + 16)
                pool.tensor_tensor(xres[:, :, :], xres[:, :, :],
                                       bv[:, BV["out_b"]:BV["out_b"] + D].unsqueeze(1).to_broadcast((P, TILES, D)),
                                       ALU.add).then_inc(xb_sb, 1)

            def rstd(dst, ve, done):
                pool.tensor_tensor(dst[:, :], ve[:, :], expo[:, 0:TILES], ALU.pow).then_inc(done, 1)

            def mamba_norm(g):
                pool.wait_ge(m_var, at(m_var, g))
                rstd(m_rs, m_ve, m_rstd)

            def take_x1(g):
                pool.wait_ge(x1_sb, at(x1_sb, g))
                for dst in (xf, x1c):
                    pool.tensor_tensor(dst[:, :, :], x1[:, :, :],
                                           zero[:, :].unsqueeze(1).to_broadcast((P, TILES, D)), ALU.add).then_inc(x1_taken, 1)

            def rope(g, l, i):
                n = l * TILES + i
                pool.wait_ge(ssc_sb, at(ssc_sb, g, n + 1))
                if i > 0 or l > 0:
                    pool.wait_ge(qk_sb, at(qk_sb, g, n))
                pool.wait_ge(v_sb, at(v_sb, g, n + 1))
                if l > 0:
                    pool.wait_ge(o_ps, at(o_ps, g, n - TILES + 1))
                pool.tensor_tensor(rn[:, :], ssc[:, :], expo[:, 0:2 * HEADS], ALU.pow).then_inc(rn_sb, 1)
                pool.tensor_copy(v_even[0:WIN, i, :], v_odd[0:WIN, i, :]).then_inc(ve_sb, 1)
                if i % 2 == 1:
                    pool.wait_ge(rn_sb, at(rn_sb, g, n + 1))
                    pool.wait_ge(ve_sb, at(ve_sb, g, n // 2 + n + 1))
                    pool.tensor_tensor(v_even[WIN:P, i, :], v_odd[WIN:P, i - 1, :],
                                           zero[WIN:P, 0:1].to_broadcast((WIN, INNER)), ALU.add).then_inc(ve_sb, 1)
                    pool.wait_ge(ve_sb, at(ve_sb, g, n // 2 + n + 2))
                pool.wait_ge(rope_mul, at(rope_mul, g, 2 * n + 2))
                if n >= 2:
                    pool.wait_ge(qkT_ps, at(qkT_ps, g, 2 * (n - 2) + 2))
                pool.tensor_tensor(qk[:, i % 2], qc[:, :, :], qs[:, :, :], ALU.add).then_inc(rope_add, 1)
                pool.wait_ge(rope_add, at(rope_add, g, n + 1))
                pool.wait_ge(rn_sb, at(rn_sb, g, n + 1))
                flat = qk[:, i % 2].rearrange("p a (h x) -> p (a h) x", x=DH)
                pool.tensor_tensor(flat, flat, rn[:, :].unsqueeze(2).to_broadcast((P, 2 * HEADS, DH)),
                                       ALU.mult).then_inc(qk_sb, 1)

            def ffn_norm(g, l):
                pool.wait_ge(f_var, at(f_var, g, l + 1))
                rstd(f_rs, f_ve, f_rstd)

            def ffn_bias(g, l):
                pool.wait_ge(x2_sb, at(x2_sb, g, l + 1))
                if l == 0:
                    pool.wait_ge(out_done, g * 16 + 16)
                pool.tensor_tensor(outb[:, :, :], xf[:, :, :],
                                       bv[:, BV["b2"] + l * D:BV["b2"] + (l + 1) * D].unsqueeze(1)
                                       .to_broadcast((P, TILES, D)), ALU.add).then_inc(xb2_sb, 1)

            def slot(g, l, i):
                if i < TILES:
                    rope(g, l, i)

            run(pool, {"enter": bias, "leave": mamba_norm},
                {"layer_in": lambda g, l: take_x1(g) if l == 0 else None, "slot": slot,
                 "attn_out": lambda g, l: (ffn_bias(g, l), ffn_norm(g, l)),
                 "final": lambda g: ffn_norm(g, LAYERS)})

        @block.scalar
        def _(act):
            act.wait_ge(w_in, W_IN[0])
            act.activation(negA[:, :], bv[:, BV["A_log"]:BV["A_log"] + NST], ACT.Exp).then_inc(a_exp, 1)
            act.wait_ge(setup_done, 1)
            act.wait_ge(zeros_ready, 1)

            def mamba_in(g):
                for h in range(HALF):
                    act.wait_ge(u_ps, at(u_ps, g, h + 1))
                    act.activation(upre[:, h * SEQS:(h + 1) * SEQS, TAPS - 1:], seqs(Y[h][:, :]),
                                       ACT.Identity, bias=col("in_b", h)).then_inc(upre_sb, 1)
                for h in range(HALF):
                    act.wait_ge(g_ps, at(g_ps, g, h + 1))
                    act.activation(gate[:, h * SEQS:(h + 1) * SEQS, :], seqs((M, Y[0])[h][:, :]),
                                       ACT.Identity, bias=half_gb[:, h:h + 1], scale=0.5).then_inc(gh_sb, 1)

            def mamba_silu(g):
                act.wait_ge(gh_sb, at(gh_sb, g))
                act.wait_ge(conv, at(conv, g))
                act.activation(th[:, :, :], hu[:, :, :], ACT.Tanh).then_inc(th_u, 1)
                act.wait_ge(u_sb, at(u_sb, g))
                act.activation(th[:, :, :], gate[:, :, :], ACT.Tanh).then_inc(th_g, 1)

            def mamba_rank(g):
                act.wait_ge(d1_ps, at(d1_ps, g))
                act.activation(dt1_s[:, :], M[0:RANK, :], ACT.Identity, bias=col("dt1_b", 0, RANK)).then_inc(d1_sb, 1)

            def mamba_dt(g):
                act.wait_ge(gate_sb, at(gate_sb, g))
                for h in range(HALF):
                    act.wait_ge(z_ps, at(z_ps, g, h + 1))
                    act.activation(th[:, h * SEQS:(h + 1) * SEQS, :], seqs((Y[1], M)[h][:, :]),
                                       ACT.Abs, bias=col("dt2_b", h)).then_inc(za_sb, 1)
                act.wait_ge(za_sb, at(za_sb, g))
                act.activation(th[:, :, :], th[:, :, :], ACT.Exp, scale=-1.0).then_inc(e_sb, 1)
                act.wait_ge(e_sb, at(e_sb, g))
                act.activation(th[:, :, :], th[:, :, :], ACT.Ln, bias=1.0).then_inc(l_sb, 1)

            def mamba_decay(g, n):
                if n == 0:
                    act.wait_ge(delta_sb, at(delta_sb, g))
                if n >= A_RING:
                    act.wait_ge(scan_sb, at(scan_sb, g, n - A_RING + 1))
                act.activation(decay[:, n % A_RING, :, 1:], delta[:, :, :], ACT.Exp,
                                   scale=negA[:, n:n + 1]).then_inc(decay_sb, 1)

            def layer_in(g, l):
                act.wait_ge(ht_ps, at(ht_ps, g, l + 1))
                act.activation(hT[0:D // 2, :, :], seqs(F[2][0:D // 2, :]), ACT.Copy)
                act.activation(hT[D // 2:D, :, 1:], seqs(F[2][D // 2:D, :])[:, :, 0:SEQ - 1], ACT.Copy).then_inc(ht_sb, 1)

            def squares(g, l, i):
                n = l * TILES + i
                if n:
                    act.wait_ge(ss_sb, at(ss_sb, g, n))
                for a in range(2):
                    act.wait_ge(qkv_ps, at(qkv_ps, g, 3 * n + a + 1))
                    act.activation(sq[:, a, :], F[a][:, :], ACT.Square).then_inc(sq_sb, 1)
                act.wait_ge(qkv_ps, at(qkv_ps, g, 3 * n + 3))
                if l > 0:
                    act.wait_ge(o_ps, at(o_ps, g, n - TILES + 1))
                    act.wait_ge(ve_sb, at(ve_sb, g, TILES + TILES // 2))
                act.activation(v_odd[:, i, :], F[2][:, :], ACT.Copy).then_inc(v_sb, 1)

            def probs_T(g, l, i):
                n = l * TILES + i
                act.wait_ge(pT_ps, at(pT_ps, g, 2 * n + 2))
                if n:
                    act.wait_ge(o_ps, at(o_ps, g, n))
                act.activation(probT[:, 1::2, :], F[4][:, :].rearrange("p (h x) -> p h x", x=P), ACT.Copy).then_inc(pTo_sb, 1)

            def qk_T(g, l, i):
                n = l * TILES + i
                s, j = i // 2, i % 2
                if n >= 2:
                    act.wait_ge(s_ps, at(s_ps, g, 2 * n - 2))
                act.wait_ge(qkT_ps, at(qkT_ps, g, 2 * n + 1))
                act.activation(qT[:, i % 2], F[3][:, :].rearrange("p (c x) -> p c x", x=P), ACT.Copy).then_inc(qkT_sb, 1)
                act.wait_ge(qkT_ps, at(qkT_ps, g, 2 * n + 2))
                act.activation(kT[:, s, :, WIN + j * P:WIN + (j + 1) * P],
                                   F[4][:, :].rearrange("p (c x) -> p c x", x=P), ACT.Copy).then_inc(qkT_sb, 1)

            def softmax(g, l, i):
                n = l * TILES + i
                if n:
                    act.wait_ge(pT_ps, at(pT_ps, g, 2 * n))
                if n >= 2:
                    act.wait_ge(rden_sb, at(rden_sb, g, n - 1))
                for a in range(2):
                    act.wait_ge(nmax_sb, at(nmax_sb, g, 2 * n + a + 1))
                    for c in range(PAIRS):
                        h = 2 * c + a
                        ins = act.activation(prob[:, h, :], F[3 + a][:, c * P:(c + 1) * P], ACT.Exp,
                                             bias=nmax[:, i % 2, h:h + 1], accum_out=den[:, i % 2, h:h + 1])
                    ins.then_inc(prob_sb, 1)

            def out_T(g, l, i):
                n = l * TILES + i
                act.wait_ge(oT_ps, at(oT_ps, g, n + 1))
                if l > 0:
                    act.wait_ge(wo_ps, at(wo_ps, g, l))
                act.activation(oT[:, i], F[2][:, :].rearrange("p (c x) -> p c x", x=P), ACT.Copy).then_inc(oT_sb, 1)

            def norm_T(g, l):
                act.wait_ge(hnT_ps, at(hnT_ps, g, l + 1))
                act.activation(hnT[:, :], F[1][:, :], ACT.Identity, bias=col("ln_b", l),
                                   scale=col("ln_g", l)).then_inc(hnT_sb, 1)

            def gelus(g, l):
                if l > 0:
                    act.wait_ge(w2_ps, at(w2_ps, g, l))
                for c, (_, n) in enumerate(CH):
                    k = l * NCH + c
                    act.wait_ge(up_ps, at(up_ps, g, 2 * k + 1))
                    act.activation(hid[0:n, c, :], F[(3, 0, 2)[c]][0:n, :], ACT.Gelu,
                                       bias=col("b1g", l * NCH + c, n)).then_inc(gelu_sb, 1)

            def slot(g, l, s):
                if s < TILES:
                    squares(g, l, s)
                if 0 <= s - 2:
                    probs_T(g, l, s - 2)
                if 0 <= s - 1 < TILES:
                    qk_T(g, l, s - 1)
                    softmax(g, l, s - 1)
                if 0 <= s - 2:
                    out_T(g, l, s - 2)

            run(act, {"enter": mamba_in, "activate": mamba_silu, "rank": mamba_rank, "step_size": mamba_dt,
                      "state": mamba_decay},
                {"layer_in": layer_in, "slot": slot, "attn_out": norm_T, "ffn": gelus})

        @block.vector
        def _(dve):
            def once(ins, count=[0]):
                count[0] += 1
                ins.then_inc(setup, 1)
                dve.wait_ge(setup, count[0])

            dve.memset(zero[:, :], 0.0)
            dve.memset(u[:, :, 0:1], 0.0)
            dve.memset(du[:, :, 0:1], 0.0)
            dve.memset(decay[:, :, :, 0:1], 0.0)
            dve.memset(upre[:, :, 0:TAPS - 1], 0.0)
            dve.memset(hT[:, :, 0:1], 0.0)
            dve.memset(kT[:, :, :, 0:WIN], 0.0)
            dve.memset(v_even[:, :, :], 0.0).then_inc(zeros_ready, 1)
            dve.wait_ge(w_in, W_IN[0])
            dve.wait_ge(zeros_ready, 1)
            dve.wait_ge(a_exp, 1)
            once(dve.tensor_scalar(tiny[:, :], negA[:, :], TINY_A, None, ALU.is_lt))
            once(dve.tensor_reduce(any_tiny[:, :], tiny[:, :], AX.X, ALU.max))
            once(dve.tensor_copy(flag[:, :], any_tiny[:, :]))
            once(dve.tensor_scalar(none_tiny[:, :], any_tiny[:, :], -1.0, 1.0, ALU.mult, ALU.add))
            once(dve.tensor_scalar(negA[:, :], negA[:, :], -1.0, None, ALU.mult))
            once(dve.tensor_scalar(halfA[:, :], negA[:, :], 0.5, None, ALU.mult))
            once(dve.tensor_scalar(keep[:, :], tiny[:, :], -1.0, 1.0, ALU.mult, ALU.add))
            once(dve.tensor_tensor(rA[:, :], negA[:, :], keep[:, :], ALU.mult))
            once(dve.tensor_tensor(rA[:, :], rA[:, :], tiny[:, :], ALU.add))
            once(dve.reciprocal(rA[:, :], rA[:, :]))
            once(dve.tensor_tensor(expand[:, :], rA[:, :], keep[:, :], ALU.mult))
            once(dve.tensor_scalar(rA[:, :], rA[:, :], none_tiny[:, :], any_tiny[:, :], ALU.mult, ALU.add))
            w = wsum[:, :, 0:NST]
            once(dve.tensor_tensor(w, pv[:, PV["B"]:PV["B"] + HALF * NST].rearrange("p (h n) -> p h n", h=HALF),
                                   pv[:, PV["C"]:PV["C"] + HALF * NST].rearrange("p (h n) -> p h n", h=HALF), ALU.mult))
            once(dve.tensor_tensor(w, w, rA[:, :].unsqueeze(1).to_broadcast((P, HALF, NST)), ALU.mult))
            once(dve.tensor_reduce(wsum[:, :, NST], w, AX.X, ALU.add))
            once(dve.tensor_scalar(wsum[:, :, NST], wsum[:, :, NST], none_tiny[:, :], None, ALU.mult))
            once(dve.tensor_tensor(wsum[:, :, NST], pv[:, PV["D"]:PV["D"] + HALF], wsum[:, :, NST], ALU.subtract))
            for h in range(HALF):
                for n in range(NST + 1):
                    ins = dve.tensor_scalar(diag[:, h, n, :], ident[:, :], wsum[:, h, n:n + 1], None, ALU.mult)
            once(ins)
            once(dve.tensor_copy(identb[:, :], ident[:, :]))
            once(dve.tensor_copy(mask[:, :, :], prob[:, 0:2, :]))
            once(dve.tensor_scalar(half_cw[:, :], pv[:, PV["conv_w"]:PV["conv_w"] + HALF * TAPS], 0.5, None, ALU.mult))
            once(dve.tensor_scalar(half_cb[:, :], pv[:, PV["conv_b"]:PV["conv_b"] + HALF], 0.5, None, ALU.mult))
            once(dve.tensor_scalar(half_gb[:, :], pv[:, PV["gate_b"]:PV["gate_b"] + HALF], 0.5, None, ALU.mult))
            for l in range(LAYERS):
                for j in range(2):
                    sc = bv[:, BV["qk_scale"] + l * 2 * DH:BV["qk_scale"] + (l + 1) * 2 * DH].rearrange(
                        "p (a x) -> p a x", a=2)
                    once(dve.tensor_tensor(rope_c[:, l, j], rope_c[:, l, j], sc, ALU.mult))
                    for b in range(2):
                        lo, hi = b * DH // 2, (b + 1) * DH // 2
                        other = slice((1 - b) * DH // 2, (2 - b) * DH // 2)
                        once(dve.tensor_tensor(rope_s[:, l, j, :, lo:hi], rope_s[:, l, j, :, lo:hi],
                                               sc[:, :, other], ALU.mult))
            dve.engine_nop().then_inc(setup_done, 1)
            dve.engine_nop().then_inc(out_done, 16)
            has_tiny = dve.value_load(flag[0:1, 0:1], min_val=0, max_val=1)

            def convolve(g):
                for h in range(HALF):
                    ab = slice(h * SEQS, (h + 1) * SEQS)
                    dve.wait_ge(upre_sb, at(upre_sb, g, h + 1))
                    k = h * TAPS
                    dve.tensor_scalar(hu[:, ab, :], upre[:, ab, 0:SEQ], half_cw[:, k:k + 1], half_cb[:, h:h + 1],
                                          ALU.mult, ALU.add).then_inc(conv, 1)
                    for c in range(1, TAPS):
                        dve.wait_ge(conv, at(conv, g, k + c))
                        dve.scalar_tensor_tensor(out=hu[:, ab, :], in0=upre[:, ab, c:c + SEQ],
                                                     scalar=half_cw[:, k + c:k + c + 1], in1=hu[:, ab, :],
                                                     op0=ALU.mult, op1=ALU.add).then_inc(conv, 1)

            def activate(g):
                dve.wait_ge(th_u, at(th_u, g))
                dve.scalar_tensor_tensor(out=u[:, :, 1:], in0=th[:, :, :], scalar=1.0, in1=hu[:, :, :],
                                             op0=ALU.add, op1=ALU.mult).then_inc(u_sb, 1)
                dve.wait_ge(th_g, at(th_g, g))
                dve.scalar_tensor_tensor(out=gate[:, :, :], in0=th[:, :, :], scalar=1.0, in1=gate[:, :, :],
                                             op0=ALU.add, op1=ALU.mult).then_inc(gate_sb, 1)
                dve.wait_ge(u_sb, at(u_sb, g))
                dve.tensor_tensor(du[:, :, 1:], u[:, :, 1:], u[:, :, 0:SEQ], ALU.subtract).then_inc(du_sb, 1)

            def step_size(g):
                for h in range(HALF):
                    dve.wait_ge(za_sb, at(za_sb, g, h + 1))
                    dve.tensor_scalar(hu[:, h * SEQS:(h + 1) * SEQS, :], seqs((Y[1], M)[h][:, :]),
                                          col("dt2_b", h), 0.0, ALU.add, ALU.max).then_inc(zr_sb, 1)
                dve.wait_ge(l_sb, at(l_sb, g))
                dve.wait_ge(zr_sb, at(zr_sb, g))
                dve.tensor_tensor(delta[:, :, :], hu[:, :, :], th[:, :, :], ALU.add).then_inc(delta_sb, 1)

            def scan_state(g, n):
                def inputs_ready():
                    if n == 0:
                        dve.wait_ge(du_sb, at(du_sb, g))
                    dve.wait_ge(decay_sb, at(decay_sb, g, n + 1))
                    if n >= R_RING:
                        dve.wait_ge(scan_used, at(scan_used, g, n - R_RING + 1))

                state = scan[:, n % R_RING].rearrange("p a l -> p (a l)")
                a = decay[:, n % A_RING]
                with dve.If(has_tiny == 0):
                    inputs_ready()
                    dve.tensor_tensor_scan(state, du[:, :, :].rearrange("p a l -> p (a l)"),
                                               a.rearrange("p a l -> p (a l)"), 0.0, ALU.add, ALU.mult).then_inc(scan_sb, 1)
                with dve.Else():
                    inputs_ready()
                    dve.tensor_scalar(hu[:, :, :], delta[:, :, :], halfA[:, n:n + 1], 1.0, ALU.mult, ALU.add).then_inc(series, 1)
                    dve.wait_ge(series, at(series, g, 5 * n + 1))
                    dve.scalar_tensor_tensor(out=hu[:, :, :], in0=hu[:, :, :], scalar=tiny[:, n:n + 1],
                                                 in1=delta[:, :, :], op0=ALU.mult, op1=ALU.mult).then_inc(series, 1)
                    dve.tensor_scalar(th[:, :, :], a[:, :, 1:], 1.0, expand[:, n:n + 1], ALU.subtract, ALU.mult).then_inc(series, 1)
                    dve.wait_ge(series, at(series, g, 5 * n + 3))
                    dve.tensor_tensor(hu[:, :, :], hu[:, :, :], th[:, :, :], ALU.add).then_inc(series, 1)
                    dve.wait_ge(series, at(series, g, 5 * n + 4))
                    dve.tensor_tensor(du[:, :, 1:], hu[:, :, :], u[:, :, 1:], ALU.mult).then_inc(series, 1)
                    dve.wait_ge(series, at(series, g, 5 * n + 5))
                    dve.tensor_tensor_scan(state, a.rearrange("p a l -> p (a l)"),
                                               du[:, :, :].rearrange("p a l -> p (a l)"), 0.0, ALU.mult, ALU.add).then_inc(scan_sb, 1)

            def gated(g):
                for h in range(HALF):
                    dve.wait_ge(y_ps, at(y_ps, g, h + 1))
                    ab = slice(h * SEQS, (h + 1) * SEQS)
                    dve.tensor_tensor(gate[:, ab, :], seqs(Y[h][:, :]), gate[:, ab, :], ALU.mult).then_inc(yg_sb, 1)

            def normalise(dst, src, mv, rs, sig):
                for i in range(TILES):
                    ins = dve.tensor_scalar(dst[:, i, :], src[:, i, :], mv[:, i, 0:1], rs[:, i:i + 1],
                                            ALU.subtract, ALU.mult)
                ins.then_inc(sig, 1)

            def mamba_out(g):
                dve.wait_ge(mo_ps, at(mo_ps, g))
                dve.wait_ge(xb_sb, at(xb_sb, g))
                dve.tensor_tensor(xres[:, :, :], M[:, :].rearrange("p (t d) -> p t d", d=D), xres[:, :, :],
                                      ALU.add).then_inc(m_sum, 1)
                dve.wait_ge(m_sum, at(m_sum, g))
                for i in range(TILES):
                    ins = dve.bn_stats(m_st[:, i, :], xres[:, i, :])
                ins.then_inc(m_stat, 1)
                dve.wait_ge(m_stat, at(m_stat, g))
                dve.memset(tick[:, :], 0.0)
                for i in range(TILES):
                    ins = dve.bn_aggr(m_mv[:, i, :], m_st[:, i, :])
                ins.then_inc(m_aggr, 1)
                dve.wait_ge(m_aggr, at(m_aggr, g))
                dve.tensor_scalar(m_ve[:, :], m_mv[:, :, 1], EPS, None, ALU.add).then_inc(m_var, 1)
                dve.wait_ge(m_rstd, at(m_rstd, g))
                if not (isinstance(g, int) and g == 0):
                    dve.wait_ge(x1_taken, at(x1_taken, g, 0))
                normalise(x1, xres, m_mv, m_rs, x1_sb)

            def rope(g, l, i):
                n = l * TILES + i
                dve.wait_ge(sq_sb, at(sq_sb, g, 2 * n + 2))
                if n:
                    dve.wait_ge(ssc_sb, at(ssc_sb, g, n))
                dve.tensor_reduce(ss[:, :], sq[:, :, :].rearrange("p a (h x) -> p (a h) x", x=DH), AX.X, ALU.add).then_inc(ss_sb, 1)
                dve.wait_ge(ss_sb, at(ss_sb, g, n + 1))
                if n:
                    dve.wait_ge(rn_sb, at(rn_sb, g, n))
                dve.tensor_scalar(ssc[:, :], ss[:, :], 1e-24, None, ALU.max).then_inc(ssc_sb, 1)
                if n:
                    dve.wait_ge(rope_add, at(rope_add, g, n))
                for a in range(2):
                    src = F[a][:, :].rearrange("p (h x) -> p h x", x=DH)
                    swap = F[a][:, :].rearrange("p (h b x) -> p h b x", b=2, x=DH // 2)[:, :, ::-1, :]
                    cos = rope_c[:, l, i % 2, a, :].unsqueeze(1).to_broadcast((P, HEADS, DH))
                    sin = rope_s[:, l, i % 2, a, :].rearrange("p (b x) -> p b x", b=2).unsqueeze(1)\
                        .to_broadcast((P, HEADS, 2, DH // 2))
                    dve.tensor_tensor(qc[:, a, :].rearrange("p (h x) -> p h x", x=DH), src, cos, ALU.mult)
                    dve.tensor_tensor(qs[:, a, :].rearrange("p (h b x) -> p h b x", b=2, x=DH // 2),
                                          swap, sin, ALU.mult).then_inc(rope_mul, 1)

            def probs_T(g, l, i):
                n = l * TILES + i
                dve.wait_ge(pT_ps, at(pT_ps, g, 2 * n + 1))
                if n:
                    dve.wait_ge(o_ps, at(o_ps, g, n))
                dve.tensor_copy(probT[:, 0::2, :], F[3][:, :].rearrange("p (h x) -> p h x", x=P)).then_inc(pTe_sb, 1)
                dve.wait_ge(prob_sb, at(prob_sb, g, 2 * n + 2))
                if n:
                    dve.wait_ge(o_sb, at(o_sb, g, n))
                dve.reciprocal(rden[:, :], den[:, i % 2, :]).then_inc(rden_sb, 1)

            def attended(g, l, i):
                n = l * TILES + i
                dve.wait_ge(o_ps, at(o_ps, g, n + 1))
                dve.wait_ge(rden_sb, at(rden_sb, g, n + 1))
                if n:
                    dve.wait_ge(oT_ps, at(oT_ps, g, n))
                dve.tensor_tensor(o_s[:, :].rearrange("p (h x) -> p h x", x=DH),
                                      F[2][:, :].rearrange("p (h x) -> p h x", x=DH),
                                      rden[:, :].unsqueeze(2).to_broadcast((P, HEADS, DH)), ALU.mult).then_inc(o_sb, 1)

            def row_max(g, l, i):
                n = l * TILES + i
                if n >= 2:
                    dve.wait_ge(prob_sb, at(prob_sb, g, 2 * (n - 1)))
                for a in range(2):
                    dve.wait_ge(s_ps, at(s_ps, g, 2 * n + a + 1))
                    dve.tensor_reduce(nmax[:, i % 2, a::2], F[3 + a][:, :].rearrange("p (c x) -> p c x", x=P),
                                          AX.X, ALU.max, negate=True).then_inc(nmax_sb, 1)

            def attn_out(g, l):
                dve.wait_ge(wo_ps, at(wo_ps, g, l + 1))
                dve.tensor_tensor(xf[:, :, :], F[2][:, :].rearrange("p (t d) -> p t d", d=D), xf[:, :, :],
                                      ALU.add).then_inc(x2_sb, 1)
                dve.wait_ge(x2_sb, at(x2_sb, g, l + 1))
                dve.wait_ge(sh_ps, at(sh_ps, g, l + 1))
                late = F[0][:, 0:TILES * D // 2].rearrange("p (t d) -> p t d", t=TILES)
                for i in range(TILES):
                    dve.bn_stats(f_st[:, i, 0, :], xf[:, i, 0:D // 2])
                    ins = dve.bn_stats(f_st[:, i, 1, :], late[:, i, :])
                ins.then_inc(f_stat, 1)
                dve.wait_ge(f_stat, at(f_stat, g, l + 1))
                dve.memset(tick[:, :], 0.0)
                for i in range(TILES):
                    ins = dve.bn_aggr(f_mv[:, i, :], f_st[:, i, :, :].rearrange("p a b -> p (a b)"))
                ins.then_inc(f_aggr, 1)
                dve.wait_ge(f_aggr, at(f_aggr, g, l + 1))
                dve.tensor_scalar(f_ve[:, :], f_mv[:, :, 1], EPS, None, ALU.add).then_inc(f_var, 1)
                dve.wait_ge(f_rstd, at(f_rstd, g, l + 1))
                for i in range(TILES):
                    dve.tensor_scalar(hn[:, i, 0:D // 2], xf[:, i, 0:D // 2], f_mv[:, i, 0:1], f_rs[:, i:i + 1],
                                      ALU.subtract, ALU.mult)
                    ins = dve.tensor_scalar(hn[:, i, D // 2:], late[:, i, :], f_mv[:, i, 0:1], f_rs[:, i:i + 1],
                                            ALU.subtract, ALU.mult)
                ins.then_inc(hn_sb, 1)

            def hidden(g, l):
                for c, (_, n) in enumerate(CH):
                    k = l * NCH + c
                    dve.wait_ge(up_ps, at(up_ps, g, 2 * k + 2))
                    dve.wait_ge(gelu_sb, at(gelu_sb, g, k + 1))
                    dve.scalar_tensor_tensor(out=hid[0:n, c, :], in0=F[(4, 1, 3)[c]][0:n, :],
                                                 scalar=col("b1a", l * NCH + c, n), in1=hid[0:n, c, :],
                                                 op0=ALU.add, op1=ALU.mult).then_inc(hid_sb, 1)
                dve.wait_ge(w2_ps, at(w2_ps, g, l + 1))
                dve.wait_ge(xb2_sb, at(xb2_sb, g, l + 1))
                dve.tensor_tensor(xf[:, :, :], F[4][:, :].rearrange("p (t d) -> p t d", d=D), outb[:, :, :],
                                      ALU.add).then_inc(x3_sb, 1)

            def final(g):
                dve.wait_ge(x3_sb, at(x3_sb, g))
                dve.wait_ge(x1_taken, at(x1_taken, g))
                dve.tensor_tensor(x1c[:, :, :], x1c[:, :, :], xf[:, :, :], ALU.add).then_inc(z_sum, 1)
                dve.wait_ge(z_sum, at(z_sum, g))
                for i in range(TILES):
                    ins = dve.bn_stats(f_st[:, i, 0, :], x1c[:, i, :])
                ins.then_inc(z_stat, 1)
                dve.wait_ge(z_stat, at(z_stat, g))
                dve.memset(tick[:, :], 0.0)
                for i in range(TILES):
                    ins = dve.bn_aggr(f_mv[:, i, :], f_st[:, i, 0, :])
                ins.then_inc(f_aggr, 1)
                dve.wait_ge(f_aggr, at(f_aggr, g))
                dve.tensor_scalar(f_ve[:, :], f_mv[:, :, 1], EPS, None, ALU.add).then_inc(f_var, 1)
                dve.wait_ge(f_rstd, at(f_rstd, g, LAYERS + 1))
                normalise(outb, x1c, f_mv, f_rs, out_sb)

            def slot(g, l, s):
                if 0 <= s - 2:
                    probs_T(g, l, s - 2)
                if s < TILES:
                    rope(g, l, s)
                if 0 <= s - 2:
                    attended(g, l, s - 2)
                if 0 <= s - 1 < TILES:
                    row_max(g, l, s - 1)

            run(dve, {"enter": convolve, "activate": activate, "step_size": step_size, "state": scan_state,
                      "leave": lambda g: (gated(g), mamba_out(g))},
                {"slot": slot, "attn_out": attn_out, "ffn": hidden, "final": final})

        @block.tensor
        def _(pe):
            pe.wait_ge(w_in, W_IN[0])
            pe.wait_ge(setup_done, 1)
            pe.wait_ge(zeros_ready, 1)

            def mm(dst, lhsT, rhs, start=True, stop=True):
                return pe.matmul(dst, lhsT, rhs, start=start, stop=stop, skip_group_check=True)

            def mamba_in(g):
                pe.wait_ge(xT_in, g * 16 + 16)
                if not (isinstance(g, int) and g == 0):
                    pe.wait_ge(yg_sb, at(yg_sb, g, 0))
                    pe.wait_ge(m_sum, at(m_sum, g, 0))
                for h in range(HALF):
                    mm(Y[h][:, :], in_w[:, h * P:(h + 1) * P], xT[:, :]).then_inc(u_ps, 1)
                for h in range(HALF):
                    if h == 1:
                        pe.wait_ge(upre_sb, at(upre_sb, g, 1))
                    mm((M, Y[0])[h][:, :], gate_w[:, h * P:(h + 1) * P], xT[:, :]).then_inc(g_ps, 1)

            def mamba_rank(g):
                pe.wait_ge(u_sb, at(u_sb, g))
                pe.wait_ge(gh_sb, at(gh_sb, g))
                for h in range(HALF):
                    ins = mm(M[0:RANK, :], dt1_w[:, h, :], u[:, h * SEQS:(h + 1) * SEQS, 1:], h == 0, h == HALF - 1)
                ins.then_inc(d1_ps, 1)

            def mamba_z(g):
                pe.wait_ge(upre_sb, at(upre_sb, g))
                pe.wait_ge(d1_sb, at(d1_sb, g))
                for h in range(HALF):
                    mm((Y[1], M)[h][:, :], dt2_w[:, h * P:(h + 1) * P], dt1_s[:, :]).then_inc(z_ps, 1)

            def mamba_skip(g):
                pe.wait_ge(zr_sb, at(zr_sb, g))
                for h in range(HALF):
                    mm(Y[h][:, :], diag[:, h, NST, :], u[:, h * SEQS:(h + 1) * SEQS, 1:], True, False)

            def mamba_y(g, n):
                pe.wait_ge(scan_sb, at(scan_sb, g, n + 1))
                for h in range(HALF):
                    ins = mm(Y[h][:, :], diag[:, h, n, :], scan[:, n % R_RING, h * SEQS:(h + 1) * SEQS, 1:],
                             False, n == NST - 1)
                    if n == NST - 1:
                        ins.then_inc(y_ps, 1)
                if n < NST - 1:
                    ins.then_inc(scan_used, 1)

            def mamba_out(g):
                pe.wait_ge(yg_sb, at(yg_sb, g))
                for i in range(TILES):
                    s, j = i // 2, i % 2
                    for h in range(HALF):
                        ins = mm(M[:, i * D:(i + 1) * D], gate[:, h * SEQS + s, j * P:(j + 1) * P], out_w[:, h, :],
                                 h == 0, h == HALF - 1)
                ins.then_inc(mo_ps, 1)

            def layer_in(g, l):
                if l == 0:
                    pe.wait_ge(x1_taken, at(x1_taken, g, 1))
                else:
                    pe.wait_ge(x3_sb, at(x3_sb, g, l))
                for i in range(TILES):
                    ins = pe.transpose(F[2][:, i * P:(i + 1) * P], xf[:, i, :], ident[:, :])
                ins.then_inc(ht_ps, 1)

            def qkv(g, l, i):
                n = l * TILES + i
                if i == 0:
                    pe.wait_ge(ht_sb, at(ht_sb, g, l + 1))
                else:
                    pe.wait_ge(rope_mul, at(rope_mul, g, 2 * n))
                if i >= 3:
                    pe.wait_ge(oT_sb, at(oT_sb, g, n - 2))
                s, j = i // 2, i % 2
                for a in range(3):
                    if a == 2 and 0 < i < 3:
                        pe.wait_ge(v_sb, at(v_sb, g, n))
                    mm(F[a][:, :], hT[:, s, j * P:(j + 1) * P], wqkv[:, l, a * INNER:(a + 1) * INNER]).then_inc(qkv_ps, 1)

            def probs_T(g, l, i):
                n = l * TILES + i
                for a in range(2):
                    pe.wait_ge(prob_sb, at(prob_sb, g, 2 * n + a + 1))
                    for c in range(PAIRS):
                        ins = pe.transpose(F[3 + a][:, c * P:(c + 1) * P], prob[:, 2 * c + a, :], ident[:, :])
                    ins.then_inc(pT_ps, 1)

            def qk_T(g, l, i):
                n = l * TILES + i
                pe.wait_ge(qk_sb, at(qk_sb, g, n + 1))
                for a in range(2):
                    if i >= 1:
                        pe.wait_ge((pTe_sb, pTo_sb)[a], at((pTe_sb, pTo_sb)[a], g, n))
                    for c in range(PAIRS):
                        ins = pe.transpose(F[3 + a][:, c * P:(c + 1) * P], qk[:, i % 2, a, c * P:(c + 1) * P],
                                           ident[:, :])
                    ins.then_inc(qkT_ps, 1)

            def weighted(g, l, i):
                n = l * TILES + i
                pe.wait_ge(pTe_sb, at(pTe_sb, g, n + 1))
                pe.wait_ge(pTo_sb, at(pTo_sb, g, n + 1))
                pe.wait_ge(ve_sb, at(ve_sb, g, n + 1 + (n + 1) // 2))
                if i < 2:
                    pe.wait_ge(v_sb, at(v_sb, g, n + 3))
                else:
                    pe.wait_ge(oT_sb, at(oT_sb, g, n))
                for h in range(HEADS):
                    for wd in range(2):
                        v = (v_even, v_odd)[wd]
                        ins = mm(F[2][wd * WIN:(wd + 1) * WIN, h * DH:(h + 1) * DH],
                                 probT[:, h, wd * WIN:(wd + 1) * WIN], v[:, i, h * DH:(h + 1) * DH], h == 0, h == HEADS - 1)
                ins.then_inc(o_ps, 1)

            def scores(g, l, i):
                n = l * TILES + i
                s, j = i // 2, i % 2
                pe.wait_ge(qkT_sb, at(qkT_sb, g, 2 * n + 2))
                for a in range(2):
                    rows = slice(a * DH, (a + 1) * DH)
                    mm(F[3 + a][:, :], identb[:, :],
                       mask[:, j, :].unsqueeze(1).to_broadcast((P, PAIRS, P)), True, False)
                    for c in range(PAIRS):
                        for wd in range(2):
                            lo = j * P + wd * WIN
                            keys = kT[rows, s, c, lo:lo + 2 * WIN]
                            if wd == 0:
                                keys = keys.rearrange("p (b x) -> p b x", b=2)[:, ::-1, :]
                            ins = mm(F[3 + a][wd * WIN:(wd + 1) * WIN, c * P:(c + 1) * P],
                                     qT[rows, i % 2, c, wd * WIN:(wd + 1) * WIN], keys, False, c == PAIRS - 1)
                    ins.then_inc(s_ps, 1)

            def out_T(g, l, i):
                n = l * TILES + i
                pe.wait_ge(o_sb, at(o_sb, g, n + 1))
                for c in range(INNER // P):
                    ins = pe.transpose(F[2][:, c * P:(c + 1) * P], o_s[:, c * P:(c + 1) * P], ident[:, :])
                ins.then_inc(oT_ps, 1)

            def attn_out(g, l):
                pe.wait_ge(oT_sb, at(oT_sb, g, (l + 1) * TILES))
                for i in range(TILES):
                    for c in range(INNER // P):
                        ins = mm(F[2][:, i * D:(i + 1) * D], oT[:, i, c, :], wo[:, l, c, :],
                                 c == 0, c == INNER // P - 1)
                ins.then_inc(wo_ps, 1)
                pe.wait_ge(x2_sb, at(x2_sb, g, l + 1))
                for i in range(TILES):
                    dst = F[0][:, i * D // 2:(i + 1) * D // 2]
                    ins = mm(dst, shift[:, :], xf[:, i, D // 2:], True, i % 2 == 0)
                    if i % 2:
                        ins = mm(dst, carry[:, :], xf[:, i - 1, D // 2:], False, True)
                ins.then_inc(sh_ps, 1)
                pe.wait_ge(hn_sb, at(hn_sb, g, l + 1))
                for i in range(TILES):
                    ins = pe.transpose(F[1][:, i * P:(i + 1) * P], hn[:, i, :], ident[:, :])
                ins.then_inc(hnT_ps, 1)

            def ffn(g, l):
                pe.wait_ge(hnT_sb, at(hnT_sb, g, l + 1))
                pe.wait_ge(pTe_sb, at(pTe_sb, g, (l + 1) * TILES))
                pe.wait_ge(pTo_sb, at(pTo_sb, g, (l + 1) * TILES))
                for c, (lo, n) in enumerate(CH):
                    if c == 2:
                        pe.wait_ge(gelu_sb, at(gelu_sb, g, l * NCH + 1))
                    mm(F[(3, 0, 2)[c]][0:n, :], w1[:, l, HID + lo:HID + lo + n], hnT[:, :]).then_inc(up_ps, 1)
                    mm(F[(4, 1, 3)[c]][0:n, :], w1[:, l, lo:lo + n], hnT[:, :]).then_inc(up_ps, 1)
                pe.wait_ge(hid_sb, at(hid_sb, g, (l + 1) * NCH))
                for i in range(TILES):
                    for c, (lo, n) in enumerate(CH):
                        ins = mm(F[4][:, i * D:(i + 1) * D], hid[0:n, c, i * P:(i + 1) * P], w2[0:n, l, c, :],
                                 c == 0, c == NCH - 1)
                ins.then_inc(w2_ps, 1)

            def slot(g, l, s):
                if s < TILES:
                    qkv(g, l, s)
                if 0 <= s - 2:
                    probs_T(g, l, s - 2)
                if 0 <= s - 1 < TILES:
                    qk_T(g, l, s - 1)
                if 0 <= s - 2:
                    weighted(g, l, s - 2)
                if 0 <= s - 1 < TILES:
                    scores(g, l, s - 1)
                if 0 <= s - 2:
                    out_T(g, l, s - 2)

            run(pe, {"enter": mamba_in, "rank": mamba_rank, "step_size": mamba_z, "skip": mamba_skip,
                     "state": mamba_y, "leave": mamba_out},
                {"layer_in": layer_in, "slot": slot, "attn_out": attn_out, "ffn": ffn})


def _consts():
    import numpy as np
    half = np.arange(0, DH, 2, dtype=np.float32)
    inv = (np.float32(1.0) / np.float32(10000.0) ** (half / np.float32(DH))).astype(np.float32)
    tt = np.arange(SEQ, dtype=np.float32)
    fr = tt[:, None] * inv[None, :]
    fr = np.concatenate([fr, fr], -1)
    base = (half + np.float32(0.4 * DH)) / np.float32(1.4 * DH)
    power = (tt - SEQ // 2) / np.float32(WIN // 2)
    scale = base[None, :].astype(np.float32) ** power[:, None]
    scale = np.concatenate([scale, scale], -1)
    sign = np.where(np.arange(DH) < DH // 2, -1.0, 1.0).astype(np.float32)
    cos, sin = np.cos(fr), np.sin(fr) * sign
    c = np.stack([cos * scale * QK_SCALE, cos / scale], 1)
    s = np.stack([sin * scale * QK_SCALE, sin / scale], 1)
    tile = lambda a: np.ascontiguousarray(a.reshape(2, P, 2, DH).transpose(1, 0, 2, 3)).astype(np.float32)
    i = np.arange(WIN)[:, None]
    j = np.arange(WIN)[None, :]
    own, before = j <= i, j >= i
    mask = np.zeros((P, 2, P), bool)
    mask[:WIN, 1] = np.concatenate([own, before], 1)
    mask[:WIN, 0] = np.concatenate([own, np.zeros_like(before)], 1)
    mask[WIN:, 0] = mask[WIN:, 1] = np.concatenate([before, own], 1)
    eye = np.eye(P, dtype=np.float32)
    carry = np.zeros((P, P), np.float32)
    carry[P - 1, 0] = 1.0
    return {"rope_c": tile(c), "rope_s": tile(s), "ident": eye, 
            "shift": np.eye(P, k=1, dtype=np.float32), "carry": carry,
            "mask": np.where(mask, 0.0, MASKED).astype(np.float32)}


def kernel(**inputs):
    import numpy as np
    import concourse.bacc as bacc
    from concourse.bass_utils import run_bass_kernel_spmd

    a = {k: np.ascontiguousarray(v) for k, v in inputs.items()}
    m = {k[len("L0_attn_"):]: v for k, v in a.items() if k.startswith("L0_attn_")}
    f = {k[len("L0_ffn_"):]: v for k, v in a.items() if k.startswith("L0_ffn_")}

    def halves(v):
        return v.reshape(HALF, P, -1).transpose(1, 0, 2).reshape(P, -1)

    def chunks(v):
        r = np.zeros((LAYERS, NCH * P), np.float32)
        r[:, :HID] = v
        return r.reshape(LAYERS * NCH, P).T

    dt1_b = np.zeros((P, 1), np.float32)
    dt1_b[:RANK, 0] = m["dt1_b"]
    x = m["x"].reshape(GROUPS, TOK, D)
    arrays = {
        "x": x, "xT": x.transpose(0, 2, 1),
        "pv": np.concatenate([halves(m["in_b"]), halves(m["gate_b"]), halves(m["conv_b"]),
                              halves(m["conv_w"].reshape(DI, TAPS)), halves(m["D_vec"]), dt1_b, halves(m["dt2_b"]),
                              halves(m["B_mat"].T), halves(m["C_mat"].T), f["ln_g"].T, f["ln_b"].T,
                              chunks(f["b1"][:, :HID]), chunks(f["b1"][:, HID:])], 1),
        "bv": np.concatenate([m["A_log"], m["out_b"],
                              np.stack([f["q_scale"], f["k_scale"]], 1).reshape(-1), f["b2"].reshape(-1)]),
        "in_w": m["in_w"], "gate_w": m["gate_w"], "dt1_w": m["dt1_w"], "dt2_w": m["dt2_w"], "out_w": m["out_w"],
        "wqkv": f["wqkv"], "wo": f["wo"], "w1": f["w1"], "w2": f["w2"], **_consts()}
    arrays = {f"in_{k}": np.ascontiguousarray(v) for k, v in arrays.items()}

    nc = bacc.Bacc("TRN2", target_bir_lowering=False, num_devices=1)
    t = {k[3:]: nc.dram_tensor(k, v.shape, mybir.dt.from_np(v.dtype), kind="ExternalInput").ap()
         for k, v in arrays.items()}
    out = nc.dram_tensor("out", (GROUPS, TOK, D), F32, kind="ExternalOutput").ap()
    build(nc, t, out)
    r = run_bass_kernel_spmd(nc, [arrays], core_ids=[0])
    return r.results[0]["out"].reshape(BATCH, SEQ, D)
```
